# Optimizing a Trainium2 kernel written in Bass

```python
import numpy as np
import jax
import jax.numpy as jnp

def _softmax(x, axis=-1):
    return jax.nn.softmax(x, axis=axis)

def _gelu(x):
    return jax.nn.gelu(x, approximate=True)

def _silu(x):
    return jax.nn.silu(x)

def _sigmoid(x):
    return jax.nn.sigmoid(x)

def _layernorm(x, axis=-1, eps=1e-05):
    m = jnp.mean(x, axis=axis, keepdims=True)
    v = jnp.var(x, axis=axis, keepdims=True)
    return (x - m) / jnp.sqrt(v + eps)

def _scatter_add(tgt, idx, src, axis=0):
    return tgt.at[idx].add(src)

def _segment_sum(src, seg, n):
    return jax.ops.segment_sum(src, seg, n)
kernel_name = 'mk_dlrm_tower_d1_rec_r8_ae8f63'

def setup_inputs(seed: int=0):
    np.random.seed(seed)
    _w = jnp.asarray

    def _rec_inputs():
        import jax
        import jax.numpy as jnp
        _tk = jax.random.key(seed)
        dense_ctx = jax.random.normal(jax.random.fold_in(_tk, 190), (512, 16), jnp.float32)
        ids = jnp.stack([jax.random.randint(jax.random.fold_in(_tk, 200 + f), (512,), 0, v, jnp.int32) for f, v in enumerate([1000, 125000, 12500, 1000, 12500, 1250, 1000, 12500, 1250, 1000, 1250, 1250, 12500, 12500, 1000, 12500, 1250, 1000, 1250, 12500, 1000, 1000, 12500, 1000, 1000, 1000, 1000])], axis=1)
        tbl_0 = 0.05 * jax.random.normal(jax.random.fold_in(_tk, 500 + 0), (1000, 128), jnp.float32)
        tbl_1 = 0.05 * jax.random.normal(jax.random.fold_in(_tk, 500 + 1), (125000, 128), jnp.float32)
        tbl_2 = 0.05 * jax.random.normal(jax.random.fold_in(_tk, 500 + 2), (12500, 128), jnp.float32)
        tbl_3 = 0.05 * jax.random.normal(jax.random.fold_in(_tk, 500 + 3), (1000, 128), jnp.float32)
        tbl_4 = 0.05 * jax.random.normal(jax.random.fold_in(_tk, 500 + 4), (12500, 128), jnp.float32)
        tbl_5 = 0.05 * jax.random.normal(jax.random.fold_in(_tk, 500 + 5), (1250, 128), jnp.float32)
        tbl_6 = 0.05 * jax.random.normal(jax.random.fold_in(_tk, 500 + 6), (1000, 128), jnp.float32)
        tbl_7 = 0.05 * jax.random.normal(jax.random.fold_in(_tk, 500 + 7), (12500, 128), jnp.float32)
        tbl_8 = 0.05 * jax.random.normal(jax.random.fold_in(_tk, 500 + 8), (1250, 128), jnp.float32)
        tbl_9 = 0.05 * jax.random.normal(jax.random.fold_in(_tk, 500 + 9), (1000, 128), jnp.float32)
        tbl_10 = 0.05 * jax.random.normal(jax.random.fold_in(_tk, 500 + 10), (1250, 128), jnp.float32)
        tbl_11 = 0.05 * jax.random.normal(jax.random.fold_in(_tk, 500 + 11), (1250, 128), jnp.float32)
        tbl_12 = 0.05 * jax.random.normal(jax.random.fold_in(_tk, 500 + 12), (12500, 128), jnp.float32)
        tbl_13 = 0.05 * jax.random.normal(jax.random.fold_in(_tk, 500 + 13), (12500, 128), jnp.float32)
        tbl_14 = 0.05 * jax.random.normal(jax.random.fold_in(_tk, 500 + 14), (1000, 128), jnp.float32)
        tbl_15 = 0.05 * jax.random.normal(jax.random.fold_in(_tk, 500 + 15), (12500, 128), jnp.float32)
        tbl_16 = 0.05 * jax.random.normal(jax.random.fold_in(_tk, 500 + 16), (1250, 128), jnp.float32)
        tbl_17 = 0.05 * jax.random.normal(jax.random.fold_in(_tk, 500 + 17), (1000, 128), jnp.float32)
        tbl_18 = 0.05 * jax.random.normal(jax.random.fold_in(_tk, 500 + 18), (1250, 128), jnp.float32)
        tbl_19 = 0.05 * jax.random.normal(jax.random.fold_in(_tk, 500 + 19), (12500, 128), jnp.float32)
        tbl_20 = 0.05 * jax.random.normal(jax.random.fold_in(_tk, 500 + 20), (1000, 128), jnp.float32)
        tbl_21 = 0.05 * jax.random.normal(jax.random.fold_in(_tk, 500 + 21), (1000, 128), jnp.float32)
        tbl_22 = 0.05 * jax.random.normal(jax.random.fold_in(_tk, 500 + 22), (12500, 128), jnp.float32)
        tbl_23 = 0.05 * jax.random.normal(jax.random.fold_in(_tk, 500 + 23), (1000, 128), jnp.float32)
        tbl_24 = 0.05 * jax.random.normal(jax.random.fold_in(_tk, 500 + 24), (1000, 128), jnp.float32)
        tbl_25 = 0.05 * jax.random.normal(jax.random.fold_in(_tk, 500 + 25), (1000, 128), jnp.float32)
        tbl_26 = 0.05 * jax.random.normal(jax.random.fold_in(_tk, 500 + 26), (1000, 128), jnp.float32)
        _rk = jax.random.fold_in(_tk, 7)
        W_top1 = 0.0521996 * jax.random.normal(jax.random.fold_in(_tk, 801), (367, 512), jnp.float32)
        W_top2 = 0.0441942 * jax.random.normal(jax.random.fold_in(_tk, 802), (512, 256), jnp.float32)
        W_top3 = 0.0625 * jax.random.normal(jax.random.fold_in(_tk, 803), (256, 1), jnp.float32)
        b_top1 = jnp.zeros((512,), jnp.float32)
        b_top2 = jnp.zeros((256,), jnp.float32)
        return (dense_ctx, ids, tbl_0, tbl_1, tbl_2, tbl_3, tbl_4, tbl_5, tbl_6, tbl_7, tbl_8, tbl_9, tbl_10, tbl_11, tbl_12, tbl_13, tbl_14, tbl_15, tbl_16, tbl_17, tbl_18, tbl_19, tbl_20, tbl_21, tbl_22, tbl_23, tbl_24, tbl_25, tbl_26, W_top1, b_top1, W_top2, b_top2, W_top3)
    dense_ctx, ids, tbl_0, tbl_1, tbl_2, tbl_3, tbl_4, tbl_5, tbl_6, tbl_7, tbl_8, tbl_9, tbl_10, tbl_11, tbl_12, tbl_13, tbl_14, tbl_15, tbl_16, tbl_17, tbl_18, tbl_19, tbl_20, tbl_21, tbl_22, tbl_23, tbl_24, tbl_25, tbl_26, W_top1, b_top1, W_top2, b_top2, W_top3 = _rec_inputs()

    def _L0_rec_setup():
        import jax, jax.numpy as jnp
        import numpy as np
        B, F, D = (2048, 27, 128)
        _TRIL_I, _TRIL_J = np.tril_indices(F, k=-1)
        key = jax.random.key(seed)
        features = jax.random.normal(key, (B, F, D), dtype=jnp.float32)
        return {'features': features}
    _L0_rec_all = _L0_rec_setup()
    _L0_rec_in = {k: v for k, v in _L0_rec_all.items() if k in ()}
    del _L0_rec_all
    return {'dense_ctx': dense_ctx, 'ids': ids, 'tbl_0': tbl_0, 'tbl_1': tbl_1, 'tbl_2': tbl_2, 'tbl_3': tbl_3, 'tbl_4': tbl_4, 'tbl_5': tbl_5, 'tbl_6': tbl_6, 'tbl_7': tbl_7, 'tbl_8': tbl_8, 'tbl_9': tbl_9, 'tbl_10': tbl_10, 'tbl_11': tbl_11, 'tbl_12': tbl_12, 'tbl_13': tbl_13, 'tbl_14': tbl_14, 'tbl_15': tbl_15, 'tbl_16': tbl_16, 'tbl_17': tbl_17, 'tbl_18': tbl_18, 'tbl_19': tbl_19, 'tbl_20': tbl_20, 'tbl_21': tbl_21, 'tbl_22': tbl_22, 'tbl_23': tbl_23, 'tbl_24': tbl_24, 'tbl_25': tbl_25, 'tbl_26': tbl_26, 'W_top1': W_top1, 'b_top1': b_top1, 'W_top2': W_top2, 'b_top2': b_top2, 'W_top3': W_top3}

def reference(dense_ctx, ids, tbl_0, tbl_1, tbl_2, tbl_3, tbl_4, tbl_5, tbl_6, tbl_7, tbl_8, tbl_9, tbl_10, tbl_11, tbl_12, tbl_13, tbl_14, tbl_15, tbl_16, tbl_17, tbl_18, tbl_19, tbl_20, tbl_21, tbl_22, tbl_23, tbl_24, tbl_25, tbl_26, W_top1, b_top1, W_top2, b_top2, W_top3):
    import jax
    import jax.numpy as jnp

    def _L0_rec_ref(features):
        import jax, jax.numpy as jnp
        import numpy as np
        B, F, D = (2048, 27, 128)
        _TRIL_I, _TRIL_J = np.tril_indices(F, k=-1)
        xactions = jnp.einsum('bfd,bgd->bfg', features, features)
        activations = xactions[:, _TRIL_I, _TRIL_J]
        return activations
    e = jnp.stack([tbl_0[ids[:, 0]], tbl_1[ids[:, 1]], tbl_2[ids[:, 2]], tbl_3[ids[:, 3]], tbl_4[ids[:, 4]], tbl_5[ids[:, 5]], tbl_6[ids[:, 6]], tbl_7[ids[:, 7]], tbl_8[ids[:, 8]], tbl_9[ids[:, 9]], tbl_10[ids[:, 10]], tbl_11[ids[:, 11]], tbl_12[ids[:, 12]], tbl_13[ids[:, 13]], tbl_14[ids[:, 14]], tbl_15[ids[:, 15]], tbl_16[ids[:, 16]], tbl_17[ids[:, 17]], tbl_18[ids[:, 18]], tbl_19[ids[:, 19]], tbl_20[ids[:, 20]], tbl_21[ids[:, 21]], tbl_22[ids[:, 22]], tbl_23[ids[:, 23]], tbl_24[ids[:, 24]], tbl_25[ids[:, 25]], tbl_26[ids[:, 26]]], axis=1)
    z = _L0_rec_ref(e)
    z = z.reshape(z.shape[0], -1)
    h = jnp.concatenate([z, dense_ctx], axis=1)
    h = jnp.maximum(h @ W_top1 + b_top1, 0.0)
    h = jnp.maximum(h @ W_top2 + b_top2, 0.0)
    y = h @ W_top3
    return y

_drawn_inputs = setup_inputs


def setup_inputs(seed=0):
    import zlib

    import numpy as np

    out = dict(_drawn_inputs(seed))
    spreads = {'b_top1': (0.0, 0.1), 'b_top2': (0.0, 0.1)}
    factors = {}
    for name, (base, spread) in spreads.items():
        noise = np.random.default_rng([zlib.crc32(name.encode()), seed]).standard_normal(out[name].shape)
        drawn = base * np.exp(spread * noise) if base else spread * noise
        out[name] = jnp.asarray(drawn.astype(out[name].dtype))
    for name, factor in factors.items():
        out[name] = (out[name] * factor).astype(out[name].dtype)
    return out
```

```python
from contextlib import ExitStack

import concourse.bass as bass
from concourse import mybir

F32 = mybir.dt.float32
I32 = mybir.dt.int32
U32 = mybir.dt.uint32
ALU = mybir.AluOpType
ACT = mybir.ActivationFunctionType

P = 128
DMA = 16
FEATURES = 27
GROUP = 4
GROUPS = [list(range(f, min(f + GROUP, FEATURES))) for f in range(0, FEATURES, GROUP)]
ID_HALF = 16
SIDE = FEATURES - 1
PER_BANK = 16


def pair_of(i):
    return i * (i - 1) // 2


def build(nc, dense_ctx, ids, tables, W_top1, b_top1, W_top2, b_top2, W_top3, y):
    batch, n_dense = dense_ctx.shape
    d = tables[0].shape[1]
    n_in, n_h1 = W_top1.shape
    n_h2 = W_top2.shape[1]
    pairs = pair_of(FEATURES)
    tiles = batch // P
    k1 = [(k, min(P, n_in - k)) for k in range(0, n_in, P)]
    m1, m2 = n_h1 // P, n_h2 // P
    half1 = m1 // 2
    zt_cut = len(k1) - 1
    k_last = k1[-1][1]
    rounds = P // PER_BANK
    assert m2 == 2 and d == P and n_in == pairs + n_dense and tables[0].shape[1] == d
    dve_groups = (len(GROUPS) + 1) // 2
    act_groups = len(GROUPS) // 2
    half_rounds = rounds // 2

    with ExitStack() as ctx:
        def sb(name, shape, dt=F32):
            return ctx.enter_context(nc.sbuf_tensor(name, shape, dt))

        def ps(name, shape):
            return ctx.enter_context(nc.psum_tensor(name, shape, F32))

        def sem(name):
            return ctx.enter_context(nc.semaphore(name))

        ident = sb("ident", [P, P])
        ids_sb = sb("ids_sb", [P, FEATURES], I32)
        X = sb("X", [P, FEATURES, d])
        ET = sb("ET", [P, P, FEATURES])
        G = sb("G", [SIDE, SIDE, P])
        Z = sb("Z", [P, n_in])
        ZT = sb("ZT", [P, len(k1), P])
        h1T = sb("h1T", [P, m1, P])
        h2T = sb("h2T", [P, m2, P])
        w1 = sb("w1", [P, len(k1), n_h1])
        w2 = sb("w2", [P, m1, n_h2])
        w3 = sb("w3", [P, m2])
        b1 = sb("b1", [P, m1])
        b2 = sb("b2", [P, m2])
        y_sb = sb("y_sb", [P, tiles])

        ps_t = [ps(f"ps_t{i}", [P, GROUP, P]) for i in range(2)]
        ps_g = [ps(f"ps_g{i}", [P, 512]) for i in range(2)]
        ps_m = [ps(f"ps_m{i}", [P, 4, P]) for i in range(4)]
        ps_z = ps_m[0][:, :, :].rearrange("p a b -> p (a b)")
        ps_zt = [ps_m[1], ps_m[0]]
        ps_h1 = [ps_m[2], ps_m[3]]
        ps_h2 = [ps_m[0], ps_m[1]]
        ps_y = ps_m[2]

        ident_zero, ident_ready = sem("ident_zero"), sem("ident_ready")
        ids_in = [sem("ids_lo_in"), sem("ids_hi_in")]
        half_begun = sem("half_begun")
        x_in = [sem(f"x_in{g}") for g in range(len(GROUPS))]
        dense_in, w1_in, w2_in, small_in = sem("dense_in"), sem("w1_in"), sem("w2_in"), sem("small_in")
        turned = [sem(f"turned{g}") for g in range(len(GROUPS))]
        et_dve, et_act = sem("et_dve"), sem("et_act")
        dots = sem("dots")
        g_dve, g_act = sem("g_dve"), sem("g_act")
        z_laid = sem("z_laid")
        z_kept = sem("z_kept")
        z_turned = sem("z_turned")
        zt_dve, zt_act = sem("zt_dve"), sem("zt_act")
        h1_done = sem("h1_done")
        h1_dve, h1_act = sem("h1_dve"), sem("h1_act")
        h2_done = sem("h2_done")
        h2_dve, h2_act = sem("h2_dve"), sem("h2_act")
        y_done, y_kept, y_out = sem("y_done"), sem("y_kept"), sem("y_out")

        ids_tiles = ids.rearrange("(p t) f -> t p f", t=tiles)
        dense_tiles = dense_ctx.rearrange("(p t) c -> t p c", t=tiles)

        block = ctx.enter_context(nc.Block())

        @block.sync
        def _(sp):
            halves = [slice(0, ID_HALF), slice(ID_HALF, FEATURES)]
            last_group = [ID_HALF // GROUP - 1, len(GROUPS) - 1]
            for h in range(2):
                sp.dma_start(ids_sb[:, halves[h]], ids_tiles[0, :, halves[h]]).then_inc(ids_in[h], DMA)
            sp.dma_start(Z[:, pairs:n_in], dense_tiles[0, :, :]).then_inc(dense_in, DMA)
            with sp.Fori(1, tiles) as t:
                for h in range(2):
                    for g in range(last_group[h], last_group[0] if h else -1, -1):
                        sp.wait_ge(x_in[g], t * (DMA * len(GROUPS[g])))
                    sp.dma_start(ids_sb[:, halves[h]], ids_tiles[t, :, halves[h]]).then_inc(ids_in[h], DMA)
                sp.wait_ge(z_turned, t)
                sp.dma_start(Z[:, pairs:n_in], dense_tiles[t, :, :]).then_inc(dense_in, DMA)
            sp.wait_ge(y_kept, tiles)
            sp.dma_start(y.rearrange("(p t) o -> p (t o)", t=tiles), y_sb[:, :]).then_inc(y_out, DMA)
            sp.wait_ge(y_out, DMA)

        @block.gpsimd
        def _(pool):
            pool.memset(ident[:, :], 0.0).then_inc(ident_zero, 1)
            pool.wait_ge(ident_zero, 1)
            pool.affine_select(out=ident[:, :], in_=ident[:, :], compare_op=ALU.not_equal, fill=1.0,
                               base=0, pattern=[[-1, P]], channel_multiplier=1).then_inc(ident_ready, 1)
            with pool.Fori(1, tiles + 1) as count:
                for g, group in enumerate(GROUPS):
                    if group[0] % ID_HALF == 0:
                        half = group[0] // ID_HALF
                        pool.wait_ge(ids_in[half], count * DMA)
                        pool.sem_inc(half_begun, 1)
                    pool.wait_ge(ident_ready, 1)
                    pool.wait_ge(turned[g], count)
                    for f in group:
                        pool.indirect_dma_start(
                            out=X[:, f, :], out_offset=None, in_=tables[f][:, :],
                            in_offset=bass.IndirectOffsetOnAxis(ap=ids_sb[:, f:f + 1].bitcast(U32), axis=0),
                        ).then_inc(x_in[g], DMA)


        @block.tensor
        def _(pe):
            for g in range(len(GROUPS)):
                pe.sem_inc(turned[g], 1)
            pe.wait_ge(ident_ready, 1)
            pe.wait_ge(w1_in, len(k1) * DMA)
            pe.wait_ge(w2_in, DMA)
            pe.wait_ge(small_in, 3 * DMA)
            with pe.Fori(0, tiles) as t:
                for g, group in enumerate(GROUPS):
                    pe.wait_ge(x_in[g], t * (DMA * len(group)) + DMA * len(group))
                    if g % 2 == 0:
                        pe.wait_ge(et_dve, t * dve_groups + (g // 2 + 1))
                    else:
                        pe.wait_ge(et_act, t * act_groups + (g // 2 + 1))
                    for n, f in enumerate(group):
                        last = pe.transpose(ps_t[g % 2][:, n, :], X[:, f, :], ident[:, :])
                    last.then_inc(turned[g], 1)
                pe.wait_ge(et_dve, t * dve_groups + (dve_groups + 1))
                pe.wait_ge(et_act, t * act_groups + (act_groups + 1))
                for r in range(rounds):
                    if r % 2 == 0:
                        pe.wait_ge(g_dve, t * half_rounds + (r // 2 + 1))
                    else:
                        pe.wait_ge(g_act, t * half_rounds + (r // 2 + 1))
                    for n in range(PER_BANK):
                        p = r * PER_BANK + n
                        last = pe.matmul(ps_g[r % 2][0:SIDE, n * SIDE:(n + 1) * SIDE], ET[:, p, 0:SIDE],
                                         ET[:, p, 1:FEATURES], start=True, stop=True)
                    last.then_inc(dots, 1)
                pe.wait_ge(ident_ready, 1)
                pe.wait_ge(g_dve, t * half_rounds + (half_rounds + 1))
                pe.wait_ge(g_act, t * half_rounds + (half_rounds + 1))
                for i in range(1, FEATURES):
                    last = pe.transpose(ps_z[:, pair_of(i):pair_of(i + 1)], G[0:i, i - 1, :], ident[0:i, 0:i])
                last.then_inc(z_laid, 1)
                pe.wait_ge(z_kept, t + 1)
                pe.wait_ge(dense_in, t * DMA + DMA)
                for c, (k, kn) in enumerate(k1):
                    bank, slot = (ps_zt[0], c) if c < zt_cut else (ps_zt[1], 0)
                    last = pe.transpose(bank[0:kn, slot, :], Z[:, k:k + kn], ident[:, :])
                last.then_inc(z_turned, 1)
                pe.wait_ge(zt_dve, t + 1)
                pe.wait_ge(zt_act, t + 1)
                for m in range(m1):
                    for c, (k, kn) in enumerate(k1):
                        last = pe.matmul(ps_h1[m // half1][:, m % half1, :], w1[0:kn, c, m * P:(m + 1) * P], ZT[0:kn, c, :],
                                         start=(c == 0), stop=(c == len(k1) - 1))
                    if m % half1 == half1 - 1:
                        last.then_inc(h1_done, 1)
                pe.wait_ge(h1_act, t * half1 + half1)
                pe.wait_ge(h1_dve, t * half1 + half1)
                for m in range(m2):
                    for c in range(m1):
                        last = pe.matmul(ps_h2[m][:, 0, :], w2[:, c, m * P:(m + 1) * P], h1T[:, c, :],
                                         start=(c == 0), stop=(c == m1 - 1))
                    last.then_inc(h2_done, 1)
                pe.wait_ge(h2_act, t + 1)
                pe.wait_ge(h2_dve, t + 1)
                for c in range(m2):
                    last = pe.matmul(ps_y[:, 0, 0:1], h2T[:, c, :], w3[:, c:c + 1],
                                     start=(c == 0), stop=(c == m2 - 1))
                last.then_inc(y_done, 1)

        def et_group(g):
            a, n = GROUPS[g][0], len(GROUPS[g])
            return ET[:, :, a:a + n].rearrange("d p f -> d f p"), ps_t[g % 2][:, 0:n, :]

        def g_round(r):
            to = G[:, :, r * PER_BANK:(r + 1) * PER_BANK].rearrange("j i p -> j p i")
            return to, ps_g[r % 2][0:SIDE, 0:PER_BANK * SIDE].rearrange("j (p i) -> j p i", i=SIDE)

        @block.vector
        def _(dve):
            dve.sem_inc(et_dve, 1)
            dve.sem_inc(g_dve, 1)
            with dve.Fori(0, tiles) as t:
                for g in range(0, len(GROUPS), 2):
                    dve.wait_ge(turned[g], t + 2)
                    dve.tensor_copy(*et_group(g)).then_inc(et_dve, 1)
                for r in range(0, rounds, 2):
                    dve.wait_ge(dots, t * rounds + r + 1)
                    dve.tensor_copy(*g_round(r)).then_inc(g_dve, 1)
                dve.wait_ge(z_laid, t + 1)
                dve.tensor_copy(Z[:, 0:pairs], ps_z[:, 0:pairs]).then_inc(z_kept, 1)
                dve.wait_ge(z_turned, t + 1)
                dve.tensor_copy(ZT[:, 0:zt_cut, :], ps_zt[0][:, 0:zt_cut, :]).then_inc(zt_dve, 1)
                dve.wait_ge(h1_done, t * 2 + 2)
                for m in range(half1, m1):
                    dve.tensor_scalar(h1T[:, m, :], ps_h1[1][:, m - half1, :], b1[:, m:m + 1], 0.0, ALU.add, ALU.max) \
                       .then_inc(h1_dve, 1)
                dve.wait_ge(h2_done, t * m2 + 2)
                dve.tensor_scalar(h2T[:, 1, :], ps_h2[1][:, 0, :], b2[:, 1:2], 0.0, ALU.add, ALU.max) \
                   .then_inc(h2_dve, 1)
                dve.wait_ge(y_done, t + 1)
                dve.tensor_copy(y_sb[:, bass.ds(t, 1)], ps_y[:, 0, 0:1]).then_inc(y_kept, 1)

        @block.scalar
        def _(act):
            act.sem_inc(et_act, 1)
            act.sem_inc(g_act, 1)
            for c, (k, kn) in enumerate(k1):
                act.dma_start(w1[0:kn, c, :], W_top1[k:k + kn, :]).then_inc(w1_in, DMA)
            act.dma_start(w2[:, :, :], W_top2.rearrange("(c p) n -> p c n", p=P)).then_inc(w2_in, DMA)
            with nc.allow_non_contiguous_dma(reason="biases and W_top3, one value per partition"):
                act.dma_start(b1[:, :], b_top1.rearrange("(m p) -> p m", p=P)).then_inc(small_in, DMA)
                act.dma_start(b2[:, :], b_top2.rearrange("(m p) -> p m", p=P)).then_inc(small_in, DMA)
                act.dma_start(w3[:, :], W_top3.rearrange("(m p) o -> p (m o)", p=P)).then_inc(small_in, DMA)
            with act.Fori(0, tiles) as t:
                for g in range(1, len(GROUPS), 2):
                    act.wait_ge(turned[g], t + 2)
                    act.copy(*et_group(g)).then_inc(et_act, 1)
                for r in range(1, rounds, 2):
                    act.wait_ge(dots, t * rounds + r + 1)
                    act.copy(*g_round(r)).then_inc(g_act, 1)
                act.wait_ge(z_turned, t + 1)
                act.copy(ZT[0:k_last, zt_cut, :], ps_zt[1][0:k_last, 0, :]).then_inc(zt_act, 1)
                act.wait_ge(h1_done, t * 2 + 1)
                for m in range(half1):
                    act.activation(h1T[:, m, :], ps_h1[0][:, m, :], ACT.Relu, bias=b1[:, m:m + 1]).then_inc(h1_act, 1)
                act.wait_ge(h2_done, t * m2 + 1)
                act.activation(h2T[:, 0, :], ps_h2[0][:, 0, :], ACT.Relu, bias=b2[:, 0:1]).then_inc(h2_act, 1)


def kernel(**inputs):
    import numpy as np
    import concourse.bacc as bacc
    from concourse import mybir
    from concourse.bass_utils import run_bass_kernel_spmd

    nc = bacc.Bacc("TRN2", target_bir_lowering=False, num_devices=1)
    arrays, aps = {}, {}
    for name, value in inputs.items():
        value = np.ascontiguousarray(value)
        arrays[f"in_{name}"] = value
        aps[name] = nc.dram_tensor(f"in_{name}", value.shape, mybir.dt.from_np(value.dtype),
                                   kind="ExternalInput").ap()
    batch = inputs["ids"].shape[0]
    y = nc.dram_tensor("out_y", (batch, 1), mybir.dt.float32, kind="ExternalOutput").ap()
    tables = [aps[f"tbl_{f}"] for f in range(FEATURES)]
    build(nc, aps["dense_ctx"], aps["ids"], tables, aps["W_top1"], aps["b_top1"], aps["W_top2"], aps["b_top2"],
          aps["W_top3"], y)
    result = run_bass_kernel_spmd(nc, [arrays], core_ids=[0])
    return result.results[0]["out_y"]
```

```python
from contextlib import ExitStack

import concourse.bass as bass
from concourse import mybir

F32 = mybir.dt.float32
F16 = mybir.dt.float16
BF16 = mybir.dt.bfloat16
I32 = mybir.dt.int32
U32 = mybir.dt.uint32
ALU = mybir.AluOpType
ACT = mybir.ActivationFunctionType

P = 128
DMA = 16
FEATURES = 27
GROUP = 4
LOOKED_UP = [range(0, 9, 3), range(14, 20, 3)]
GATHERED = [range(1, 13, 3), range(2, 14, 3), range(9, 21, 3), range(13, 25, 3), range(23, 27), range(20, 22)]
FIRST = ["u0", "u1", "u2", "g0", "u3", "g1", "u4", "g2", "g3", "g4", "g5"]
LAST_LOOK_UP = 3
SIDE = FEATURES - 1
PER_BANK = 16
CHUNKS = 8


def pair_of(i):
    return i * (i - 1) // 2


def span(group):
    return slice(group[0], group[-1] + 1, group.step)


def build(nc, dense_ctx, ids, tables, W_top1, b_top1, W_top2, b_top2, W_top3, y):
    batch, n_dense = dense_ctx.shape
    d = tables[0].shape[1]
    n_in, n_h1 = W_top1.shape
    n_h2 = W_top2.shape[1]
    pairs = pair_of(FEATURES)
    tiles = batch // P
    k1 = [(k, min(P, n_in - k)) for k in range(0, n_in, P)]
    m1, m2 = n_h1 // P, n_h2 // P
    half1 = m1 // 2
    zt_cut = len(k1) - 1
    k_last = k1[-1][1]
    rounds = P // PER_BANK
    half_rounds = rounds // 2
    assert m2 == 2 and d == P and n_in == pairs + n_dense

    looked = [f for group in LOOKED_UP for f in group]
    gathered = [f for group in GATHERED for f in group]
    assert sorted(looked + gathered) == list(range(FEATURES))
    rows = tables[looked[0]].shape[0]
    assert all(tables[f].shape[0] == rows for f in looked) and rows % CHUNKS == 0 and rows <= 2048
    V = rows // CHUNKS
    V16 = V // 16 * 16
    dve_banks = (len(GATHERED) + 1) // 2
    act_banks = len(GATHERED) // 2
    n_look = len(looked)
    group_of = [g for g, group in enumerate(LOOKED_UP) for _ in group]
    place_of = [n for group in LOOKED_UP for n in range(len(group))]

    with ExitStack() as ctx:
        def sb(name, shape, dt=F32):
            return ctx.enter_context(nc.sbuf_tensor(name, shape, dt))

        def ps(name, shape):
            return ctx.enter_context(nc.psum_tensor(name, shape, F32))

        def sem(name):
            return ctx.enter_context(nc.semaphore(name))

        ident = sb("ident", [P, P])
        ident16 = sb("ident16", [P, P], F16)
        vocab_col = sb("vocab_col", [V, CHUNKS], I32)
        vocab = sb("vocab", [V, CHUNKS, P], F16)
        ids_all = sb("ids_all", [P, tiles, FEATURES], I32)
        ids16 = sb("ids16", [P, n_look, tiles], F16)
        ids_row = sb("ids_row", [V, n_look, batch], F16)
        onehot = sb("onehot", [V, n_look, CHUNKS, P], BF16)
        tbl = sb("tbl", [V, n_look, CHUNKS, d])
        rest = sb("rest", [V, n_look, CHUNKS, d])
        third = sb("third", [V, n_look, CHUNKS, d], BF16)
        X = sb("X", [P, 2, len(gathered), d])
        ET = sb("ET", [P, P, FEATURES])
        G = sb("G", [SIDE, SIDE, P])
        Z = sb("Z", [P, n_in])
        ZT = sb("ZT", [P, len(k1), P])
        h1T = sb("h1T", [P, m1, P])
        h2T = sb("h2T", [P, m2, P])
        w1 = sb("w1", [P, len(k1), n_h1])
        w2 = sb("w2", [P, m1, n_h2])
        w3 = sb("w3", [P, m2])
        b1 = sb("b1", [P, m1])
        b2 = sb("b2", [P, m2])
        y_sb = sb("y_sb", [P, tiles])

        ps_x = [ps(f"ps_x{i}", [P, GROUP, P]) for i in range(2)]
        ps_l = [ps(f"ps_l{i}", [P, GROUP, P]) for i in range(2)]
        ps_g = [ps(f"ps_g{i}", [P, GROUP, P]) for i in range(2)]
        ps_m = [ps(f"ps_m{i}", [P, GROUP, P]) for i in range(2)]
        ps_z = ps_m[0][:, :, :].rearrange("p a b -> p (a b)")
        ps_zt = ps_m
        ps_h1 = ps_g
        ps_h2 = ps_m
        ps_y = ps_g[0]
        ps_ids = [*ps_x, *ps_l, *ps_g]
        def high(x):
            return x.bitcast(BF16)[:, 1::2]

        ident_zero, ident_ready, ident16_ready = sem("ident_zero"), sem("ident_ready"), sem("ident16_ready")
        numbered, vocab_ready = sem("numbered"), sem("vocab_ready")
        ids_in, ids16_ready = sem("ids_in"), sem("ids16_ready")
        ids_spread = sem("ids_spread")
        row_ready = sem("row_ready")
        tbl_in = [sem(f"tbl_in{k}") for k in range(n_look)]
        rest_ready, third_ready = sem("rest_ready"), sem("third_ready")
        onehot_ready = sem("onehot_ready")
        looked_up = [sem(f"looked_up{k}") for k in range(n_look)]
        x_in = [[sem(f"x_in{b}{g}") for g in range(len(GATHERED))] for b in range(2)]
        dense_in, w1_in, w2_in, small_in = sem("dense_in"), sem("w1_in"), sem("w2_in"), sem("small_in")
        turned = [sem(f"turned{g}") for g in range(len(GATHERED))]
        et_x = [sem("et_x_dve"), sem("et_x_act")]
        et_l = [sem("et_l_dve"), sem("et_l_act")]
        dots = sem("dots")
        g_dve, g_act = sem("g_dve"), sem("g_act")
        z_laid = sem("z_laid")
        z_kept = sem("z_kept")
        z_turned = sem("z_turned")
        zt_dve, zt_act = sem("zt_dve"), sem("zt_act")
        h1_done = sem("h1_done")
        h1_dve, h1_act = sem("h1_dve"), sem("h1_act")
        h2_done = sem("h2_done")
        h2_dve, h2_act = sem("h2_dve"), sem("h2_act")
        y_done, y_kept, y_out = sem("y_done"), sem("y_kept"), sem("y_out")

        dense_tiles = dense_ctx.rearrange("(p t) c -> t p c", t=tiles)

        block = ctx.enter_context(nc.Block())

        @block.sync
        def _(sp):
            sp.dma_start(ids_all[:, :, :], ids.rearrange("(p t) f -> p t f", t=tiles)).then_inc(ids_in, DMA)
            for k, f in enumerate(looked):
                table = tables[f].rearrange("(v c) d -> v (c d)", c=CHUNKS)
                to = tbl[:, k, :, :].rearrange("v c d -> v (c d)")
                sp.dma_start(to[0:V16, :], table[0:V16, :]).then_inc(tbl_in[k], DMA)
                sp.dma_start(to[V16:V, :], table[V16:V, :]).then_inc(tbl_in[k], DMA)
            sp.dma_start(Z[:, pairs:n_in], dense_tiles[0, :, :]).then_inc(dense_in, DMA)
            for c, (k, kn) in enumerate(k1):
                sp.dma_start(w1[0:kn, c, :], W_top1[k:k + kn, :]).then_inc(w1_in, DMA)
            sp.dma_start(w2[:, :, :], W_top2.rearrange("(c p) n -> p c n", p=P)).then_inc(w2_in, DMA)
            with sp.Fori(1, tiles) as t:
                sp.wait_ge(z_turned, t)
                sp.dma_start(Z[:, pairs:n_in], dense_tiles[t, :, :]).then_inc(dense_in, DMA)
            sp.wait_ge(y_kept, tiles)
            sp.dma_start(y.rearrange("(p t) o -> p (t o)", t=tiles), y_sb[:, :]).then_inc(y_out, DMA)
            sp.wait_ge(y_out, DMA)

        @block.gpsimd
        def _(pool):
            pool.memset(ident[:, :], 0.0).then_inc(ident_zero, 1)
            pool.iota(vocab_col[:, :], pattern=[[1, CHUNKS]], base=0, channel_multiplier=CHUNKS).then_inc(numbered, 1)
            pool.wait_ge(ident_zero, 1)
            pool.affine_select(out=ident[:, :], in_=ident[:, :], compare_op=ALU.not_equal, fill=1.0,
                               base=0, pattern=[[-1, P]], channel_multiplier=1).then_inc(ident_ready, 1)
            pool.wait_ge(ids_in, DMA)
            for t in range(tiles):
                q = 0
                for g, group in enumerate(GATHERED):
                    if t >= 2:
                        pool.wait_ge(turned[g], t - 1)
                    for f in group:
                        pool.indirect_dma_start(
                            out=X[:, t % 2, q, :], out_offset=None, in_=tables[f][:, :],
                            in_offset=bass.IndirectOffsetOnAxis(ap=ids_all[:, t, f:f + 1].bitcast(U32), axis=0),
                        ).then_inc(x_in[t % 2][g], DMA)
                        q += 1

        @block.tensor
        def _(pe):
            def look_up(k, half, t):
                g, n = group_of[k], place_of[k]
                if half == 0:
                    if n == 0 and t:
                        pe.wait_ge(et_l[g], t)
                    if t == 0:
                        pe.wait_ge(third_ready, k + 1)
                    pe.wait_ge(onehot_ready, t * n_look + k + 1)
                for c in range(half * CHUNKS // 2, (half + 1) * CHUNKS // 2):
                    for part, values in enumerate((high(tbl[:, k, c, :]), high(rest[:, k, c, :]), third[:, k, c, :])):
                        last = pe.matmul(ps_l[g][:, n, :], values, onehot[:, k, c, :],
                                         start=(c == 0 and part == 0), stop=(c == CHUNKS - 1 and part == 2))
                if half:
                    last.then_inc(looked_up[k], 1)

            def turn(g, t):
                group = GATHERED[g]
                q = sum(len(x) for x in GATHERED[:g])
                pe.wait_ge(x_in[t % 2][g], (t // 2 + 1) * DMA * len(group))
                before = t * (dve_banks, act_banks)[g % 2] + g // 2
                if before:
                    pe.wait_ge(et_x[g % 2], before)
                for n in range(len(group)):
                    last = pe.transpose(ps_x[g % 2][:, n, :], X[:, t % 2, q + n, :], ident[:, :])
                last.then_inc(turned[g], 1)

            def products(t):
                todo = [(k, half) for k in range(n_look) for half in range(2)] if t + 1 < tiles else []

                def look_up_next():
                    if todo:
                        look_up(*todo.pop(0), t + 1)

                look_up_next()
                pe.wait_ge(et_x[0], (t + 1) * dve_banks)
                pe.wait_ge(et_x[1], (t + 1) * act_banks)
                pe.wait_ge(et_l[0], t + 1)
                pe.wait_ge(et_l[1], t + 1)
                if t:
                    pe.wait_ge(y_kept, t)
                for r in range(rounds):
                    if r >= 2:
                        pe.wait_ge((g_dve, g_act)[r % 2], t * half_rounds + r // 2)
                    bank = ps_g[r % 2][:, :, :].rearrange("p a b -> p (a b)")
                    for n in range(PER_BANK):
                        p = r * PER_BANK + n
                        last = pe.matmul(bank[0:SIDE, n * SIDE:(n + 1) * SIDE], ET[:, p, 0:SIDE],
                                         ET[:, p, 1:FEATURES], start=True, stop=True)
                    last.then_inc(dots, 1)
                look_up_next()
                pe.wait_ge(g_dve, (t + 1) * half_rounds)
                pe.wait_ge(g_act, (t + 1) * half_rounds)
                for i in range(1, FEATURES):
                    last = pe.transpose(ps_z[:, pair_of(i):pair_of(i + 1)], G[0:i, i - 1, :], ident[0:i, 0:i])
                last.then_inc(z_laid, 1)
                look_up_next()
                pe.wait_ge(z_kept, t + 1)
                pe.wait_ge(dense_in, (t + 1) * DMA)
                for c, (k, kn) in enumerate(k1):
                    bank, slot = (ps_zt[0], c) if c < zt_cut else (ps_zt[1], 0)
                    last = pe.transpose(bank[0:kn, slot, :], Z[:, k:k + kn], ident[:, :])
                last.then_inc(z_turned, 1)
                look_up_next()
                pe.wait_ge(zt_dve, t + 1)
                pe.wait_ge(zt_act, t + 1)
                for m in range(m1):
                    for c, (k, kn) in enumerate(k1):
                        last = pe.matmul(ps_h1[1 - m // half1][:, m % half1, :], w1[0:kn, c, m * P:(m + 1) * P],
                                         ZT[0:kn, c, :], start=(c == 0), stop=(c == len(k1) - 1))
                    if m % half1 == half1 - 1:
                        last.then_inc(h1_done, 1)
                look_up_next()
                for half in range(2):
                    if half == 0:
                        pe.wait_ge(h1_act, (t + 1) * half1)
                    else:
                        pe.wait_ge(h1_dve, (t + 1) * half1)
                    for m in range(m2):
                        for c in range(half * half1, (half + 1) * half1):
                            last = pe.matmul(ps_h2[1 - m][:, 0, :], w2[:, c, m * P:(m + 1) * P], h1T[:, c, :],
                                             start=(c == 0), stop=(c == m1 - 1))
                        if half:
                            last.then_inc(h2_done, 1)
                look_up_next()
                pe.wait_ge(h2_act, t + 1)
                pe.wait_ge(h2_dve, t + 1)
                for c in range(m2):
                    last = pe.matmul(ps_y[:, 0, 0:1], h2T[:, c, :], w3[:, c:c + 1],
                                     start=(c == 0), stop=(c == m2 - 1))
                last.then_inc(y_done, 1)
                look_up_next()
                return todo

            pe.wait_ge(ident16_ready, 1)
            pe.wait_ge(ids16_ready, len(LOOKED_UP))
            for k in range(n_look):
                for t in range(tiles):
                    last = pe.matmul(ps_ids[k][0:V, t, :], ids16[:, k, t:t + 1].to_broadcast([P, V]), ident16[:, :],
                                     start=True, stop=True)
                last.then_inc(ids_spread, 1)
            pe.wait_ge(row_ready, n_look)
            pe.wait_ge(ident_ready, 1)
            for step in FIRST:
                if step[0] == "u":
                    look_up(int(step[1:]), 0, 0)
                    look_up(int(step[1:]), 1, 0)
                else:
                    turn(int(step[1:]), 0)
            pe.wait_ge(w1_in, len(k1) * DMA)
            pe.wait_ge(w2_in, DMA)
            pe.wait_ge(small_in, 3 * DMA)
            left = products(0)
            for t in range(1, tiles):
                for g in range(len(GATHERED)):
                    turn(g, t)
                    share = -(-len(left) // (LAST_LOOK_UP - g + 1)) if 1 <= g <= LAST_LOOK_UP else 0
                    for _ in range(share):
                        look_up(*left.pop(0), t)
                left = products(t)

        def et_part(group, bank):
            return ET[:, :, span(group)].rearrange("d p f -> d f p"), bank[:, 0:len(group), :]

        def g_round(r):
            to = G[:, :, r * PER_BANK:(r + 1) * PER_BANK].rearrange("j i p -> j p i")
            bank = ps_g[r % 2][:, :, :].rearrange("p a b -> p (a b)")
            return to, bank[0:SIDE, 0:PER_BANK * SIDE].rearrange("j (p i) -> j p i", i=SIDE)

        @block.vector
        def _(dve):
            def make_onehot(k, t):
                shape = [V, CHUNKS, P]
                mine = ids_row[:, k, bass.ds(t * P, P)].unsqueeze(1).to_broadcast(shape)
                dve.tensor_tensor(onehot[:, k, :, :], mine, vocab[:, :, :], ALU.is_equal).then_inc(onehot_ready, 1)

            def cut(k):
                def flat(x):
                    return x[:, k, :, :].rearrange("v c d -> v (c d)")
                dve.wait_ge(tbl_in[k], 2 * DMA)
                dve.tensor_tensor(flat(rest), flat(tbl), high(flat(tbl)), ALU.subtract).then_inc(rest_ready, 1)
                dve.wait_ge(rest_ready, k + 1)
                dve.tensor_tensor(flat(third), flat(rest), high(flat(rest)), ALU.subtract).then_inc(third_ready, 1)

            def keep_looked_up(t):
                dve.wait_ge(looked_up[len(LOOKED_UP[0]) - 1], t + 1)
                dve.tensor_copy(*et_part(LOOKED_UP[0], ps_l[0])).then_inc(et_l[0], 1)

            def keep_gathered(g, t):
                dve.wait_ge(turned[g], t + 1)
                dve.tensor_copy(*et_part(GATHERED[g], ps_x[0])).then_inc(et_x[0], 1)

            def make_next_first(t):
                dve.wait_ge(looked_up[0], t + 1)
                make_onehot(0, t + 1)

            def products(t, more):
                for r in range(0, rounds, 2):
                    dve.wait_ge(dots, t * rounds + (r + 1))
                    dve.tensor_copy(*g_round(r)).then_inc(g_dve, 1)
                    if more:
                        for k in range(1 + (n_look - 1) * (r // 2) // half_rounds,
                                       1 + (n_look - 1) * (r // 2 + 1) // half_rounds):
                            dve.wait_ge(looked_up[k], t + 1)
                            make_onehot(k, t + 1)
                dve.wait_ge(z_laid, t + 1)
                dve.tensor_copy(Z[:, 0:pairs], ps_z[:, 0:pairs]).then_inc(z_kept, 1)
                dve.wait_ge(z_turned, t + 1)
                dve.tensor_copy(ZT[:, 0:zt_cut, :], ps_zt[0][:, 0:zt_cut, :]).then_inc(zt_dve, 1)
                dve.wait_ge(h1_done, t * 2 + 2)
                for m in range(half1, m1):
                    dve.tensor_scalar(h1T[:, m, :], ps_h1[0][:, m - half1, :], b1[:, m:m + 1], 0.0, ALU.add, ALU.max) \
                       .then_inc(h1_dve, 1)
                dve.wait_ge(h2_done, t * m2 + 2)
                dve.tensor_scalar(h2T[:, 1, :], ps_h2[0][:, 0, :], b2[:, 1:2], 0.0, ALU.add, ALU.max) \
                   .then_inc(h2_dve, 1)
                if more:
                    keep_looked_up(t + 1)
                dve.wait_ge(y_done, t + 1)
                dve.tensor_copy(y_sb[:, bass.ds(t, 1)], ps_y[:, 0, 0:1]).then_inc(y_kept, 1)

            dve.wait_ge(ids_in, DMA)
            k = 0
            for group in LOOKED_UP:
                dve.tensor_copy(ids16[:, k:k + len(group), :],
                                ids_all[:, :, span(group)].rearrange("p t f -> p f t")).then_inc(ids16_ready, 1)
                k += len(group)
            dve.wait_ge(ident_ready, 1)
            dve.tensor_copy(ident16[:, :], ident[:, :]).then_inc(ident16_ready, 1)
            dve.wait_ge(vocab_ready, 1)
            for step in FIRST:
                n = int(step[1:])
                if step[0] == "u":
                    cut(n)
                    dve.wait_ge(row_ready, n + 1)
                    make_onehot(n, 0)
                elif n % 2 == 0:
                    keep_gathered(n, 0)
            keep_looked_up(0)
            make_next_first(0)
            dve.wait_ge(small_in, 3 * DMA)
            products(0, True)
            with dve.Fori(1, tiles - 1) as t:
                keep_gathered(0, t)
                make_next_first(t)
                for g in range(2, len(GATHERED), 2):
                    keep_gathered(g, t)
                products(t, True)
            for g in range(0, len(GATHERED), 2):
                keep_gathered(g, tiles - 1)
            products(tiles - 1, False)

        @block.scalar
        def _(act):
            def keep_looked_up(t):
                act.wait_ge(looked_up[n_look - 1], t + 1)
                act.copy(*et_part(LOOKED_UP[1], ps_l[1])).then_inc(et_l[1], 1)

            def keep_gathered(g, t):
                act.wait_ge(turned[g], t + 1)
                act.copy(*et_part(GATHERED[g], ps_x[1])).then_inc(et_x[1], 1)

            def products(t):
                for r in range(1, rounds, 2):
                    act.wait_ge(dots, t * rounds + (r + 1))
                    act.copy(*g_round(r)).then_inc(g_act, 1)
                act.wait_ge(z_turned, t + 1)
                act.copy(ZT[0:k_last, zt_cut, :], ps_zt[1][0:k_last, 0, :]).then_inc(zt_act, 1)
                act.wait_ge(h1_done, t * 2 + 1)
                for m in range(half1):
                    act.activation(h1T[:, m, :], ps_h1[1][:, m, :], ACT.Relu, bias=b1[:, m:m + 1]).then_inc(h1_act, 1)
                act.wait_ge(h2_done, t * m2 + 1)
                act.activation(h2T[:, 0, :], ps_h2[1][:, 0, :], ACT.Relu, bias=b2[:, 0:1]).then_inc(h2_act, 1)

            act.wait_ge(numbered, 1)
            act.copy(vocab[:, :, :], vocab_col[:, :].unsqueeze(2).to_broadcast([V, CHUNKS, P])).then_inc(vocab_ready, 1)
            for k in range(n_look):
                act.wait_ge(ids_spread, k + 1)
                act.copy(ids_row[:, k, :].rearrange("v (t p) -> v t p", p=P), ps_ids[k][0:V, :, :]) \
                   .then_inc(row_ready, 1)
            with nc.allow_non_contiguous_dma(reason="biases and W_top3, one value per partition"):
                act.dma_start(b1[:, :], b_top1.rearrange("(m p) -> p m", p=P)).then_inc(small_in, DMA)
                act.dma_start(b2[:, :], b_top2.rearrange("(m p) -> p m", p=P)).then_inc(small_in, DMA)
                act.dma_start(w3[:, :], W_top3.rearrange("(m p) o -> p (m o)", p=P)).then_inc(small_in, DMA)
            for step in FIRST:
                n = int(step[1:])
                if step[0] == "g" and n % 2 == 1:
                    keep_gathered(n, 0)
                elif step == f"u{n_look - 1}":
                    keep_looked_up(0)
            act.wait_ge(small_in, 3 * DMA)
            products(0)
            with act.Fori(1, tiles) as t:
                for g in range(1, len(GATHERED), 2):
                    keep_gathered(g, t)
                    if g == LAST_LOOK_UP:
                        keep_looked_up(t)
                products(t)


def kernel(**inputs):
    import numpy as np
    import concourse.bacc as bacc
    from concourse import mybir
    from concourse.bass_utils import run_bass_kernel_spmd

    nc = bacc.Bacc("TRN2", target_bir_lowering=False, num_devices=1)
    arrays, aps = {}, {}
    for name, value in inputs.items():
        value = np.ascontiguousarray(value)
        arrays[f"in_{name}"] = value
        aps[name] = nc.dram_tensor(f"in_{name}", value.shape, mybir.dt.from_np(value.dtype),
                                   kind="ExternalInput").ap()
    batch = inputs["ids"].shape[0]
    y = nc.dram_tensor("out_y", (batch, 1), mybir.dt.float32, kind="ExternalOutput").ap()
    tables = [aps[f"tbl_{f}"] for f in range(FEATURES)]
    build(nc, aps["dense_ctx"], aps["ids"], tables, aps["W_top1"], aps["b_top1"], aps["W_top2"], aps["b_top2"],
          aps["W_top3"], y)
    result = run_bass_kernel_spmd(nc, [arrays], core_ids=[0])
    return result.results[0]["out_y"]
```

```python
from contextlib import ExitStack

import concourse.bass as bass
from concourse import mybir

F32 = mybir.dt.float32
F16 = mybir.dt.float16
BF16 = mybir.dt.bfloat16
I32 = mybir.dt.int32
U32 = mybir.dt.uint32
ALU = mybir.AluOpType
ACT = mybir.ActivationFunctionType

P = 128
DMA = 16
FEATURES = 27
GROUP = 4
LOOKED_UP = [range(0, 9, 3), range(14, 20, 3)]
GATHERED = [range(1, 13, 3), range(2, 14, 3), range(9, 21, 3), range(13, 25, 3), range(23, 27), range(20, 22)]
FIRST = ["u0", "u1", "u2", "g0", "u3", "g1", "u4", "g2", "g3", "u5", "u6", "g4"]
LAST_LOOK_UP = 3
KEEP_WARM = 10
ONEHOT_ACT = (2, 3)
SIDE = FEATURES - 1
PER_BANK = 16
CHUNKS = 8


def pair_of(i):
    return i * (i - 1) // 2


def span(group):
    return slice(group[0], group[-1] + 1, group.step)


def build(nc, dense_ctx, ids, tables, W_top1, b_top1, W_top2, b_top2, W_top3, y):
    batch, n_dense = dense_ctx.shape
    d = tables[0].shape[1]
    n_in, n_h1 = W_top1.shape
    n_h2 = W_top2.shape[1]
    pairs = pair_of(FEATURES)
    tiles = batch // P
    k1 = [(k, min(P, n_in - k)) for k in range(0, n_in, P)]
    m1, m2 = n_h1 // P, n_h2 // P
    half1 = m1 // 2
    zt_cut = len(k1) - 1
    k_last = k1[-1][1]
    rounds = P // PER_BANK
    half_rounds = rounds // 2
    assert m2 == 2 and d == P and n_in == pairs + n_dense

    looked_groups = [*LOOKED_UP, GATHERED[-1]]
    looked = [f for group in looked_groups for f in group]
    gathered = [f for group in GATHERED for f in group]
    n_look = len(looked) - len(GATHERED[-1])
    assert sorted(looked[:n_look] + gathered) == list(range(FEATURES))
    rows = tables[looked[0]].shape[0]
    assert all(tables[f].shape[0] == rows for f in looked) and rows % CHUNKS == 0 and rows <= 2048
    V = rows // CHUNKS
    V16 = V // 16 * 16
    dve_banks = (len(GATHERED) + 1) // 2
    act_banks = len(GATHERED) // 2
    n_tables = len(looked)
    last_group = len(GATHERED) - 1
    group_of = [g for g, group in enumerate(looked_groups) for _ in group]
    place_of = [n for group in looked_groups for n in range(len(group))]

    with ExitStack() as ctx:
        def sb(name, shape, dt=F32):
            return ctx.enter_context(nc.sbuf_tensor(name, shape, dt))

        def ps(name, shape):
            return ctx.enter_context(nc.psum_tensor(name, shape, F32))

        def sem(name):
            return ctx.enter_context(nc.semaphore(name))

        ident = sb("ident", [P, P])
        ident16 = sb("ident16", [P, P], F16)
        vocab_col = sb("vocab_col", [V, CHUNKS], I32)
        vocab = sb("vocab", [V, CHUNKS, P], F16)
        ids_all = sb("ids_all", [P, tiles, FEATURES], I32)
        ids16 = sb("ids16", [P, n_tables, tiles], F16)
        vocab_bias = sb("vocab_bias", [V, CHUNKS])
        one = sb("one", [V, 1])
        distance = sb("distance", [V, CHUNKS, P], F16)
        ids_row = sb("ids_row", [V, n_tables, batch], F16)
        onehot = sb("onehot", [V, n_tables, CHUNKS, P], BF16)
        tbl = sb("tbl", [V, n_tables, CHUNKS, d])
        rest = sb("rest", [V, n_tables, CHUNKS, d])
        third = sb("third", [V, n_tables, CHUNKS, d], BF16)
        X = sb("X", [P, 2, len(gathered), d])
        ET = sb("ET", [P, P, FEATURES])
        G = sb("G", [SIDE, SIDE, P])
        Z = sb("Z", [P, n_in])
        ZT = sb("ZT", [P, len(k1), P])
        h1T = sb("h1T", [P, m1, P])
        h2T = sb("h2T", [P, m2, P])
        w1 = sb("w1", [P, len(k1), n_h1])
        w2 = sb("w2", [P, m1, n_h2])
        w3 = sb("w3", [P, m2])
        b1 = sb("b1", [P, m1])
        b2 = sb("b2", [P, m2])
        y_sb = sb("y_sb", [P, tiles])

        ps_x = [ps(f"ps_x{i}", [P, GROUP, P]) for i in range(2)]
        ps_l = [ps(f"ps_l{i}", [P, GROUP, P]) for i in range(2)]
        ps_g = [ps(f"ps_g{i}", [P, GROUP, P]) for i in range(2)]
        ps_m = [ps(f"ps_m{i}", [P, GROUP, P]) for i in range(2)]
        ps_z = ps_m[0][:, :, :].rearrange("p a b -> p (a b)")
        ps_zt = ps_m
        ps_h1 = ps_g
        ps_h2 = ps_m
        ps_y = ps_g[0]
        ps_look = [*ps_l, ps_x[last_group % 2]]
        ps_ids = [*ps_x, *ps_l, *ps_g, ps_m[0]]

        def high(x):
            return x.bitcast(BF16)[:, 1::2]

        one_ready = sem("one_ready")
        ident_zero, ident_ready, ident16_ready = sem("ident_zero"), sem("ident_ready"), sem("ident16_ready")
        numbered, vocab_ready = sem("numbered"), sem("vocab_ready")
        ids_in, ids16_ready = sem("ids_in"), sem("ids16_ready")
        bias_ready = sem("bias_ready")
        ids_spread = sem("ids_spread")
        row_ready = sem("row_ready")
        tbl_in = [sem(f"tbl_in{k}") for k in range(n_tables)]
        rest_ready, third_ready = sem("rest_ready"), sem("third_ready")
        onehot_ready = [sem(f"onehot_ready{k}") for k in range(n_tables)]
        distance_ready = sem("distance_ready")
        looked_up = [sem(f"looked_up{k}") for k in range(n_look)]
        x_in = [[sem(f"x_in{b}{g}") for g in range(len(GATHERED))] for b in range(2)]
        dense_in, w1_in, w2_in, small_in = sem("dense_in"), sem("w1_in"), sem("w2_in"), sem("small_in")
        turned = [sem(f"turned{g}") for g in range(len(GATHERED))]
        et_x = [sem("et_x0"), sem("et_x1")]
        et_l = [sem("et_l0"), sem("et_l1")]
        dots = sem("dots")
        g_dve, g_act = sem("g_dve"), sem("g_act")
        z_laid = sem("z_laid")
        z_kept = sem("z_kept")
        z_turned = sem("z_turned")
        zt_dve, zt_act = sem("zt_dve"), sem("zt_act")
        h1_done = sem("h1_done")
        h1_dve, h1_act = sem("h1_dve"), sem("h1_act")
        h2_done = sem("h2_done")
        h2_dve, h2_act = sem("h2_dve"), sem("h2_act")
        y_done, y_kept, y_out = sem("y_done"), sem("y_kept"), sem("y_out")

        dense_tiles = dense_ctx.rearrange("(p t) c -> t p c", t=tiles)

        block = ctx.enter_context(nc.Block())

        @block.sync
        def _(sp):
            sp.dma_start(ids_all[:, :, :], ids.rearrange("(p t) f -> p t f", t=tiles)).then_inc(ids_in, DMA)
            for k, f in enumerate(looked):
                table = tables[f].rearrange("(v c) d -> v (c d)", c=CHUNKS)
                to = tbl[:, k, :, :].rearrange("v c d -> v (c d)")
                sp.dma_start(to[0:V16, :], table[0:V16, :]).then_inc(tbl_in[k], DMA)
                sp.dma_start(to[V16:V, :], table[V16:V, :]).then_inc(tbl_in[k], DMA)
            sp.dma_start(Z[:, pairs:n_in], dense_tiles[0, :, :]).then_inc(dense_in, DMA)
            for c, (k, kn) in enumerate(k1):
                sp.dma_start(w1[0:kn, c, :], W_top1[k:k + kn, :]).then_inc(w1_in, DMA)
            sp.dma_start(w2[:, :, :], W_top2.rearrange("(c p) n -> p c n", p=P)).then_inc(w2_in, DMA)
            with sp.Fori(1, tiles) as t:
                sp.wait_ge(z_turned, t)
                sp.dma_start(Z[:, pairs:n_in], dense_tiles[t, :, :]).then_inc(dense_in, DMA)
            sp.wait_ge(y_kept, tiles)
            sp.dma_start(y.rearrange("(p t) o -> p (t o)", t=tiles), y_sb[:, :]).then_inc(y_out, DMA)
            sp.wait_ge(y_out, DMA)

        @block.gpsimd
        def _(pool):
            pool.memset(ident[:, :], 0.0).then_inc(ident_zero, 1)
            pool.iota(vocab_col[:, :], pattern=[[1, CHUNKS]], base=0, channel_multiplier=CHUNKS).then_inc(numbered, 1)
            pool.memset(one[:, :], 1.0).then_inc(one_ready, 1)
            pool.wait_ge(ident_zero, 1)
            pool.affine_select(out=ident[:, :], in_=ident[:, :], compare_op=ALU.not_equal, fill=1.0,
                               base=0, pattern=[[-1, P]], channel_multiplier=1).then_inc(ident_ready, 1)
            pool.wait_ge(ids_in, DMA)
            for t in range(tiles):
                q = 0
                for g, group in enumerate(GATHERED if t else GATHERED[:-1]):
                    if t >= 2:
                        pool.wait_ge(turned[g], t - 1)
                    for f in group:
                        pool.indirect_dma_start(
                            out=X[:, t % 2, q, :], out_offset=None, in_=tables[f][:, :],
                            in_offset=bass.IndirectOffsetOnAxis(ap=ids_all[:, t, f:f + 1].bitcast(U32), axis=0),
                        ).then_inc(x_in[t % 2][g], DMA)
                        q += 1

        @block.tensor
        def _(pe):
            def look_up(k, half, t):
                g, n = group_of[k], place_of[k]
                if half == 0:
                    if n == 0 and t:
                        pe.wait_ge(et_l[g], t)
                    if k == n_look:
                        pe.wait_ge(et_x[last_group % 2], last_group // 2)
                    if t == 0:
                        pe.wait_ge(third_ready, k + 1)
                    pe.wait_ge(onehot_ready[k], t + 1)
                for c in range(half * CHUNKS // 2, (half + 1) * CHUNKS // 2):
                    for part, values in enumerate((high(tbl[:, k, c, :]), high(rest[:, k, c, :]), third[:, k, c, :])):
                        last = pe.matmul(ps_look[g][:, n, :], values, onehot[:, k, c, :],
                                         start=(c == 0 and part == 0), stop=(c == CHUNKS - 1 and part == 2))
                if half and k < n_look:
                    last.then_inc(looked_up[k], 1)
                elif half and k == n_tables - 1:
                    last.then_inc(turned[last_group], 1)

            def turn(g, t):
                group = GATHERED[g]
                q = sum(len(x) for x in GATHERED[:g])
                loads = t // 2 + 1 if t % 2 or g < last_group else t // 2
                pe.wait_ge(x_in[t % 2][g], loads * DMA * len(group))
                before = t * (dve_banks, act_banks)[g % 2] + g // 2
                if before:
                    pe.wait_ge(et_x[g % 2], before)
                for n in range(len(group)):
                    last = pe.transpose(ps_x[g % 2][:, n, :], X[:, t % 2, q + n, :], ident[:, :])
                last.then_inc(turned[g], 1)

            def products(t):
                todo = [(k, half) for k in range(n_look) for half in range(2)] if t + 1 < tiles else []

                def look_up_next():
                    if todo:
                        look_up(*todo.pop(0), t + 1)

                def fill_wait():
                    look_up_next()
                    if t + 1 == tiles:
                        for _ in range(KEEP_WARM):
                            pe.matmul(ps_l[0][:, 0, :], ident16[:, :], ident16[:, :], start=True, stop=True)

                look_up_next()
                pe.wait_ge(et_x[0], (t + 1) * dve_banks)
                pe.wait_ge(et_x[1], (t + 1) * act_banks)
                pe.wait_ge(et_l[0], t + 1)
                pe.wait_ge(et_l[1], t + 1)
                if t:
                    pe.wait_ge(y_kept, t)
                for r in range(rounds):
                    if r >= 2:
                        pe.wait_ge((g_dve, g_act)[r % 2], t * half_rounds + r // 2)
                    bank = ps_g[r % 2][:, :, :].rearrange("p a b -> p (a b)")
                    for n in range(PER_BANK):
                        p = r * PER_BANK + n
                        last = pe.matmul(bank[0:SIDE, n * SIDE:(n + 1) * SIDE], ET[:, p, 0:SIDE],
                                         ET[:, p, 1:FEATURES], start=True, stop=True)
                    last.then_inc(dots, 1)
                fill_wait()
                pe.wait_ge(g_dve, (t + 1) * half_rounds)
                pe.wait_ge(g_act, (t + 1) * half_rounds)
                for i in range(1, FEATURES):
                    last = pe.transpose(ps_z[:, pair_of(i):pair_of(i + 1)], G[0:i, i - 1, :], ident[0:i, 0:i])
                last.then_inc(z_laid, 1)
                fill_wait()
                pe.wait_ge(z_kept, t + 1)
                pe.wait_ge(dense_in, (t + 1) * DMA)
                for c, (k, kn) in enumerate(k1):
                    bank, slot = (ps_zt[0], c) if c < zt_cut else (ps_zt[1], 0)
                    last = pe.transpose(bank[0:kn, slot, :], Z[:, k:k + kn], ident[:, :])
                last.then_inc(z_turned, 1)
                fill_wait()
                pe.wait_ge(zt_dve, t + 1)
                pe.wait_ge(zt_act, t + 1)
                for m in range(m1):
                    for c, (k, kn) in enumerate(k1):
                        last = pe.matmul(ps_h1[1 - m // half1][:, m % half1, :], w1[0:kn, c, m * P:(m + 1) * P],
                                         ZT[0:kn, c, :], start=(c == 0), stop=(c == len(k1) - 1))
                    if m % half1 == half1 - 1:
                        last.then_inc(h1_done, 1)
                look_up_next()
                for half in range(2):
                    if half == 0:
                        pe.wait_ge(h1_act, (t + 1) * half1)
                    else:
                        pe.wait_ge(h1_dve, (t + 1) * half1)
                    for m in range(m2):
                        for c in range(half * half1, (half + 1) * half1):
                            last = pe.matmul(ps_h2[1 - m][:, 0, :], w2[:, c, m * P:(m + 1) * P], h1T[:, c, :],
                                             start=(c == 0), stop=(c == m1 - 1))
                        if half:
                            last.then_inc(h2_done, 1)
                look_up_next()
                pe.wait_ge(h2_act, t + 1)
                pe.wait_ge(h2_dve, t + 1)
                for c in range(m2):
                    last = pe.matmul(ps_y[:, 0, 0:1], h2T[:, c, :], w3[:, c:c + 1],
                                     start=(c == 0), stop=(c == m2 - 1))
                last.then_inc(y_done, 1)
                look_up_next()
                return todo

            pe.wait_ge(ident16_ready, 1)
            pe.wait_ge(ids16_ready, len(looked_groups))
            for k in range(n_tables):
                for t in range(tiles):
                    last = pe.matmul(ps_ids[k][0:V, t, :], ids16[:, k, t:t + 1].to_broadcast([P, V]), ident16[:, :],
                                     start=True, stop=True)
                last.then_inc(ids_spread, 1)
            pe.wait_ge(row_ready, n_tables)
            pe.wait_ge(ident_ready, 1)
            for step in FIRST:
                if step[0] == "u":
                    look_up(int(step[1:]), 0, 0)
                    look_up(int(step[1:]), 1, 0)
                else:
                    turn(int(step[1:]), 0)
            pe.wait_ge(w1_in, len(k1) * DMA)
            pe.wait_ge(w2_in, DMA)
            pe.wait_ge(small_in, 3 * DMA)
            left = products(0)
            for t in range(1, tiles):
                for g in range(len(GATHERED)):
                    turn(g, t)
                    share = -(-len(left) // (LAST_LOOK_UP - g + 1)) if 1 <= g <= LAST_LOOK_UP else 0
                    for _ in range(share):
                        look_up(*left.pop(0), t)
                left = products(t)

        def et_part(group, bank):
            return ET[:, :, span(group)].rearrange("d p f -> d f p"), bank[:, 0:len(group), :]

        def g_round(r):
            to = G[:, :, r * PER_BANK:(r + 1) * PER_BANK].rearrange("j i p -> j p i")
            bank = ps_g[r % 2][:, :, :].rearrange("p a b -> p (a b)")
            return to, bank[0:SIDE, 0:PER_BANK * SIDE].rearrange("j (p i) -> j p i", i=SIDE)

        @block.vector
        def _(dve):
            def make_onehot(k, t):
                shape = [V, CHUNKS, P]
                mine = ids_row[:, k, bass.ds(t * P, P)].unsqueeze(1).to_broadcast(shape)
                dve.tensor_tensor(onehot[:, k, :, :], mine, vocab[:, :, :], ALU.is_equal).then_inc(onehot_ready[k], 1)

            def cut(k):
                def flat(x):
                    return x[:, k, :, :].rearrange("v c d -> v (c d)")
                dve.wait_ge(tbl_in[k], 2 * DMA)
                dve.tensor_tensor(flat(rest), flat(tbl), high(flat(tbl)), ALU.subtract).then_inc(rest_ready, 1)
                dve.wait_ge(rest_ready, k + 1)
                dve.tensor_tensor(flat(third), flat(rest), high(flat(rest)), ALU.subtract).then_inc(third_ready, 1)

            def keep_looked_up(t):
                dve.wait_ge(looked_up[len(LOOKED_UP[0]) - 1], t + 1)
                dve.tensor_copy(*et_part(LOOKED_UP[0], ps_l[0])).then_inc(et_l[0], 1)

            def keep_gathered(g, t):
                dve.wait_ge(turned[g], t + 1)
                dve.tensor_copy(*et_part(GATHERED[g], ps_x[0])).then_inc(et_x[0], 1)

            def make_next_first(t):
                dve.wait_ge(looked_up[0], t + 1)
                make_onehot(0, t + 1)

            def products(t, more):
                for r in range(0, rounds, 2):
                    dve.wait_ge(dots, t * rounds + (r + 1))
                    dve.tensor_copy(*g_round(r)).then_inc(g_dve, 1)
                    if more:
                        for k in range(1 + (n_look - 1) * (r // 2) // half_rounds,
                                       1 + (n_look - 1) * (r // 2 + 1) // half_rounds):
                            dve.wait_ge(looked_up[k], t + 1)
                            make_onehot(k, t + 1)
                dve.wait_ge(z_laid, t + 1)
                dve.tensor_copy(Z[:, 0:pairs], ps_z[:, 0:pairs]).then_inc(z_kept, 1)
                dve.wait_ge(z_turned, t + 1)
                dve.tensor_copy(ZT[:, 0:zt_cut, :], ps_zt[0][:, 0:zt_cut, :]).then_inc(zt_dve, 1)
                dve.wait_ge(h1_done, t * 2 + 2)
                for m in range(half1, m1):
                    dve.tensor_scalar(h1T[:, m, :], ps_h1[0][:, m - half1, :], b1[:, m:m + 1], 0.0, ALU.add, ALU.max) \
                       .then_inc(h1_dve, 1)
                dve.wait_ge(h2_done, t * m2 + 2)
                dve.tensor_scalar(h2T[:, 1, :], ps_h2[0][:, 0, :], b2[:, 1:2], 0.0, ALU.add, ALU.max) \
                   .then_inc(h2_dve, 1)
                if more:
                    keep_looked_up(t + 1)
                dve.wait_ge(y_done, t + 1)
                dve.tensor_copy(y_sb[:, bass.ds(t, 1)], ps_y[:, 0, 0:1]).then_inc(y_kept, 1)

            dve.wait_ge(ids_in, DMA)
            k = 0
            for group in looked_groups:
                dve.tensor_copy(ids16[:, k:k + len(group), :],
                                ids_all[:, :, span(group)].rearrange("p t f -> p f t")).then_inc(ids16_ready, 1)
                k += len(group)
            dve.wait_ge(ident_ready, 1)
            dve.tensor_copy(ident16[:, :], ident[:, :]).then_inc(ident16_ready, 1)
            dve.wait_ge(vocab_ready, 1)
            for k in range(n_tables):
                cut(k)
                if k not in ONEHOT_ACT:
                    dve.wait_ge(row_ready, k + 1)
                    make_onehot(k, 0)
            make_next_first(0)
            dve.wait_ge(small_in, 3 * DMA)
            products(0, True)
            with dve.Fori(1, tiles - 1) as t:
                keep_gathered(0, t)
                make_next_first(t)
                for g in range(2, len(GATHERED), 2):
                    keep_gathered(g, t)
                products(t, True)
            for g in range(0, len(GATHERED), 2):
                keep_gathered(g, tiles - 1)
            products(tiles - 1, False)

        @block.scalar
        def _(act):
            def keep_looked_up(g, t):
                act.wait_ge(looked_up[len(LOOKED_UP[0]) - 1 if g == 0 else n_look - 1], t + 1)
                act.copy(*et_part(LOOKED_UP[g], ps_l[g])).then_inc(et_l[g], 1)

            def keep_gathered(g, t):
                act.wait_ge(turned[g], t + 1)
                act.copy(*et_part(GATHERED[g], ps_x[g % 2])).then_inc(et_x[g % 2], 1)

            def products(t):
                for r in range(1, rounds, 2):
                    act.wait_ge(dots, t * rounds + (r + 1))
                    act.copy(*g_round(r)).then_inc(g_act, 1)
                act.wait_ge(z_turned, t + 1)
                act.copy(ZT[0:k_last, zt_cut, :], ps_zt[1][0:k_last, 0, :]).then_inc(zt_act, 1)
                act.wait_ge(h1_done, t * 2 + 1)
                for m in range(half1):
                    act.activation(h1T[:, m, :], ps_h1[1][:, m, :], ACT.Relu, bias=b1[:, m:m + 1]).then_inc(h1_act, 1)
                act.wait_ge(h2_done, t * m2 + 1)
                act.activation(h2T[:, 0, :], ps_h2[1][:, 0, :], ACT.Relu, bias=b2[:, 0:1]).then_inc(h2_act, 1)

            act.wait_ge(numbered, 1)
            act.copy(vocab_bias[:, :], vocab_col[:, :]).then_inc(bias_ready, 1)
            act.copy(vocab[:, :, :], vocab_col[:, :].unsqueeze(2).to_broadcast([V, CHUNKS, P])).then_inc(vocab_ready, 1)
            for k in range(n_tables):
                act.wait_ge(ids_spread, k + 1)
                act.copy(ids_row[:, k, :].rearrange("v (t p) -> v t p", p=P), ps_ids[k][0:V, :, :]) \
                   .then_inc(row_ready, 1)
            with nc.allow_non_contiguous_dma(reason="biases and W_top3, one value per partition"):
                act.dma_start(b1[:, :], b_top1.rearrange("(m p) -> p m", p=P)).then_inc(small_in, DMA)
                act.dma_start(b2[:, :], b_top2.rearrange("(m p) -> p m", p=P)).then_inc(small_in, DMA)
                act.dma_start(w3[:, :], W_top3.rearrange("(m p) o -> p (m o)", p=P)).then_inc(small_in, DMA)
            act.wait_ge(bias_ready, 1)
            act.wait_ge(one_ready, 1)
            for n, k in enumerate(ONEHOT_ACT):
                act.wait_ge(row_ready, k + 1)
                if n:
                    act.wait_ge(onehot_ready[ONEHOT_ACT[n - 1]], 1)
                for c in range(CHUNKS):
                    act.activation(distance[:, c, :], ids_row[:, k, 0:P], ACT.Abs, bias=vocab_bias[:, c:c + 1],
                                   scale=-1.0).then_inc(distance_ready, 1)
                act.wait_ge(distance_ready, (n + 1) * CHUNKS)
                act.activation(onehot[:, k, :, :], distance[:, :, :], ACT.Relu, bias=one[:, :], scale=-1.0) \
                   .then_inc(onehot_ready[k], 1)
            for step in FIRST:
                n = int(step[1:])
                if step[0] == "g":
                    keep_gathered(n, 0)
                elif n == n_tables - 1:
                    keep_gathered(last_group, 0)
                elif n < n_look and place_of[n] == len(LOOKED_UP[group_of[n]]) - 1:
                    keep_looked_up(group_of[n], 0)
            act.wait_ge(small_in, 3 * DMA)
            products(0)
            with act.Fori(1, tiles) as t:
                for g in range(1, len(GATHERED), 2):
                    keep_gathered(g, t)
                    if g == LAST_LOOK_UP:
                        keep_looked_up(1, t)
                products(t)


def kernel(**inputs):
    import numpy as np
    import concourse.bacc as bacc
    from concourse import mybir
    from concourse.bass_utils import run_bass_kernel_spmd

    nc = bacc.Bacc("TRN2", target_bir_lowering=False, num_devices=1)
    arrays, aps = {}, {}
    for name, value in inputs.items():
        value = np.ascontiguousarray(value)
        arrays[f"in_{name}"] = value
        aps[name] = nc.dram_tensor(f"in_{name}", value.shape, mybir.dt.from_np(value.dtype),
                                   kind="ExternalInput").ap()
    batch = inputs["ids"].shape[0]
    y = nc.dram_tensor("out_y", (batch, 1), mybir.dt.float32, kind="ExternalOutput").ap()
    tables = [aps[f"tbl_{f}"] for f in range(FEATURES)]
    build(nc, aps["dense_ctx"], aps["ids"], tables, aps["W_top1"], aps["b_top1"], aps["W_top2"], aps["b_top2"],
          aps["W_top3"], y)
    result = run_bass_kernel_spmd(nc, [arrays], core_ids=[0])
    return result.results[0]["out_y"]
```
